# Optimizing a Trainium2 kernel written in Bass

```python
import numpy as np
import jax
import jax.numpy as jnp

def _softmax(x, axis=-1):
    return jax.nn.softmax(x, axis=axis)

def _gelu(x):
    return jax.nn.gelu(x, approximate=True)

def _silu(x):
    return jax.nn.silu(x)

def _sigmoid(x):
    return jax.nn.sigmoid(x)

def _layernorm(x, axis=-1, eps=1e-05):
    m = jnp.mean(x, axis=axis, keepdims=True)
    v = jnp.var(x, axis=axis, keepdims=True)
    return (x - m) / jnp.sqrt(v + eps)

def _scatter_add(tgt, idx, src, axis=0):
    return tgt.at[idx].add(src)

def _segment_sum(src, seg, n):
    return jax.ops.segment_sum(src, seg, n)
kernel_name = 'mk_sandwich_d1_jaxref_r2_a9e720'

def setup_inputs(seed: int=0):
    np.random.seed(seed)
    _w = jnp.asarray

    def _L0_attn_setup():
        import jax, jax.numpy as jnp
        import numpy as np
        H = 16
        W = 128
        NEG = -1000000000.0
        key = jax.random.key(seed)
        k1, k2 = jax.random.split(key)
        x = jax.random.normal(k1, (4, 2048, 512), dtype=jnp.float32)
        w_qkv = jax.random.normal(k2, (512, 1536), dtype=jnp.float32) * 0.02
        return {'x': x, 'w_qkv': w_qkv}
    _L0_attn_in = _L0_attn_setup()

    def _L0_ffn_setup():
        import jax, jax.numpy as jnp
        import numpy as np
        B, S, H, F, E = (8, 1024, 512, 2048, 8)
        INIT_LAMBDA = 0.2
        key = jax.random.key(seed)
        ks = jax.random.split(key, 12)
        std = 0.02
        return {'hidden_states': jax.random.normal(ks[0], (B, S, H), jnp.float32), 'gate_w1': jax.random.normal(ks[1], (H, H), jnp.float32) * 0.01, 'gate_b1': jnp.zeros((H,), jnp.float32), 'gate_w2': jax.random.normal(ks[2], (E, H), jnp.float32) * 0.01, 'gate_b2': jnp.full((E,), INIT_LAMBDA, jnp.float32), 'W1': jax.random.normal(ks[3], (F, H), jnp.float32) * std, 'b1': jax.random.normal(ks[4], (F,), jnp.float32) * std, 'W2': jax.random.normal(ks[5], (H, F), jnp.float32) * std, 'b2': jax.random.normal(ks[6], (H,), jnp.float32) * std, 'TW1': jax.random.normal(ks[7], (E, F, H), jnp.float32) * std, 'Tb1': jax.random.normal(ks[8], (E, F), jnp.float32) * std, 'TW2': jax.random.normal(ks[9], (E, H, F), jnp.float32) * std, 'Tb2': jax.random.normal(ks[10], (E, H), jnp.float32) * std}
    _L0_ffn_in = _L0_ffn_setup()
    _d = {'L0_attn_x': _L0_attn_in['x'], 'L0_attn_w_qkv': _L0_attn_in['w_qkv'], 'L0_ffn_gate_w1': _L0_ffn_in['gate_w1'], 'L0_ffn_gate_b1': _L0_ffn_in['gate_b1'], 'L0_ffn_gate_w2': _L0_ffn_in['gate_w2'], 'L0_ffn_gate_b2': _L0_ffn_in['gate_b2'], 'L0_ffn_W1': _L0_ffn_in['W1'], 'L0_ffn_b1': _L0_ffn_in['b1'], 'L0_ffn_W2': _L0_ffn_in['W2'], 'L0_ffn_b2': _L0_ffn_in['b2'], 'L0_ffn_TW1': _L0_ffn_in['TW1'], 'L0_ffn_Tb1': _L0_ffn_in['Tb1'], 'L0_ffn_TW2': _L0_ffn_in['TW2'], 'L0_ffn_Tb2': _L0_ffn_in['Tb2']}
    _x0 = _d['L0_attn_x']
    _d['L0_attn_x'] = jax.random.normal(jax.random.fold_in(jax.random.key(seed), 1), (4, 2048, 512), dtype=_x0.dtype)
    del _x0
    return _d

def reference(L0_attn_x, L0_attn_w_qkv, L0_ffn_gate_w1, L0_ffn_gate_b1, L0_ffn_gate_w2, L0_ffn_gate_b2, L0_ffn_W1, L0_ffn_b1, L0_ffn_W2, L0_ffn_b2, L0_ffn_TW1, L0_ffn_Tb1, L0_ffn_TW2, L0_ffn_Tb2):

    def _L0_attn_ref(x, w_qkv):
        import jax, jax.numpy as jnp
        import numpy as np
        H = 16
        W = 128
        NEG = -1000000000.0
        B, L, D = x.shape
        E = D // H
        nw = L // W
        qkv = x @ w_qkv
        q, k, v = jnp.split(qkv, 3, axis=-1)

        def to_win(t):
            return t.reshape(B, L, H, E).transpose(0, 2, 1, 3).reshape(B, H, nw, W, E)
        q, k, v = map(to_win, (q, k, v))
        pad = lambda t: jnp.pad(t, ((0, 0), (0, 0), (1, 1), (0, 0), (0, 0)))
        kp, vp = (pad(k), pad(v))
        k_ctx = jnp.concatenate([kp[:, :, i:i + nw] for i in range(3)], axis=3)
        v_ctx = jnp.concatenate([vp[:, :, i:i + nw] for i in range(3)], axis=3)
        scale = E ** (-0.5)
        scores = jnp.einsum('bhnqe,bhnke->bhnqk', q * scale, k_ctx)
        key_pos = (jnp.arange(nw)[:, None] - 1) * W + jnp.arange(3 * W)[None, :]
        valid = (key_pos >= 0) & (key_pos < L)
        scores = jnp.where(valid[None, None, :, None, :], scores, NEG)
        attn = jax.nn.softmax(scores, axis=-1)
        out = jnp.einsum('bhnqk,bhnke->bhnqe', attn, v_ctx)
        return out.reshape(B, H, L, E).transpose(0, 2, 1, 3).reshape(B, L, D)

    def _L0_ffn_ref(hidden_states, gate_w1, gate_b1, gate_w2, gate_b2, W1, b1, W2, b2, TW1, Tb1, TW2, Tb2):
        import jax, jax.numpy as jnp
        import numpy as np
        B, S, H, F, E = (8, 1024, 512, 2048, 8)
        INIT_LAMBDA = 0.2
        x = hidden_states
        h = jax.nn.relu(jnp.einsum('bsh,oh->bso', x, gate_w1) + gate_b1)
        g = jnp.einsum('bso,eo->bse', h, gate_w2) + gate_b2
        g = g.mean(axis=1)
        mW1 = W1 + jnp.einsum('be,efh->bfh', g, TW1)
        mb1 = b1 + g @ Tb1
        mW2 = W2 + jnp.einsum('be,ehf->bhf', g, TW2)
        mb2 = b2 + g @ Tb2
        u = jax.nn.gelu(jnp.einsum('bsh,bfh->bsf', x, mW1) + mb1[:, None, :])
        out = jnp.einsum('bsf,bhf->bsh', u, mW2) + mb2[:, None, :]
        return out
    x = L0_attn_x
    x = x + _layernorm(_L0_attn_ref(_layernorm(x, axis=-1), L0_attn_w_qkv), axis=-1)
    x = x + _layernorm(_L0_ffn_ref(_layernorm(x, axis=-1), L0_ffn_gate_w1, L0_ffn_gate_b1, L0_ffn_gate_w2, L0_ffn_gate_b2, L0_ffn_W1, L0_ffn_b1, L0_ffn_W2, L0_ffn_b2, L0_ffn_TW1, L0_ffn_Tb1, L0_ffn_TW2, L0_ffn_Tb2), axis=-1)
    return x

_drawn_inputs = setup_inputs


def setup_inputs(seed=0):
    import zlib

    import numpy as np

    out = dict(_drawn_inputs(seed))
    spreads = {'L0_ffn_gate_b1': (0.0, 0.737), 'L0_ffn_gate_b2': (0.20000000298023224, 0.2)}
    factors = {'L0_ffn_gate_w1': 3.548, 'L0_ffn_Tb1': 4.153, 'L0_ffn_Tb2': 2.72}
    for name, (base, spread) in spreads.items():
        noise = np.random.default_rng([zlib.crc32(name.encode()), seed]).standard_normal(out[name].shape)
        drawn = base * np.exp(spread * noise) if base else spread * noise
        out[name] = jnp.asarray(drawn.astype(out[name].dtype))
    for name, factor in factors.items():
        out[name] = (out[name] * factor).astype(out[name].dtype)
    return out
```

```python
from contextlib import ExitStack

import concourse.bass as bass
from concourse import mybir

ALU = mybir.AluOpType
ACT = mybir.ActivationFunctionType
AX_X = mybir.AxisListType.X
F32 = mybir.dt.float32
F32R = mybir.dt.float32r

P = 128
D = 512
HEADS = 16
E = D // HEADS
WIN = 128
BATCH, SEQ = 4, 2048
TOKENS = BATCH * SEQ
CH = 512
TILES = CH // P
CHUNKS = TOKENS // CH
EPS = 1e-5
QH = 4
QUADS = HEADS // QH
SCALE = float(E) ** -0.5
FF = 2048
EXPERTS = 8
SLOTS = 4


def layernorm_stats(dve, x_tiles, stats, moments, chain, seen, count):
    for t in range(TILES):
        dve.bn_stats(stats[:, t, :], x_tiles[:, t, :]).then_inc(chain, 1)
    dve.wait_ge(chain, count + TILES)
    dve.sem_inc(seen, 1)
    for t in range(TILES):
        last = dve.bn_aggr(moments[:, t, :], stats[:, t, :])
    return last


def phase_qkv(nc, x, w_qkv, qk_dram, v_dram):
    KD = D // P
    PAIRS = CHUNKS // 2
    QKG = 2 * D // P
    GROUPS = QKG + TILES
    BANKS = 6
    SLOTS = 4
    with ExitStack() as ctx:
        def sb(name, shape, dt):
            return ctx.enter_context(nc.sbuf_tensor("a_" + name, shape, dt))

        def sem(name):
            return nc.alloc_semaphore("a_" + name)

        w_in = sb("w_in", [P, KD, 3 * D], F32)
        w_hi = sb("w_hi", [P, KD, 3 * D], F32R)
        w_lo = sb("w_lo", [P, KD, 3 * D], F32R)
        ident = sb("ident", [P, P], F32)
        eps = sb("eps", [P, 1], F32)
        x_in = sb("x_in", [P, 2, TILES, D], F32)
        xn = sb("xn", [P, 2, TILES, D], F32)
        xt_hi = sb("xt_hi", [P, 2, KD, CH], F32R)
        xt_lo = sb("xt_lo", [P, 2, KD, CH], F32R)
        qk = sb("qk", [P, SLOTS, 2, CH], F32R)
        v = sb("v", [P, 2, TILES, D], F32)
        stats = sb("stats", [P, TILES, 6], F32)
        moments = sb("moments", [P, TILES, 2], F32)
        std = sb("std", [P, TILES], F32)
        rstd = sb("rstd", [P, TILES], F32)
        turn = [ctx.enter_context(nc.psum_tensor(f"a_turn{i}", [P, CH], F32)) for i in range(2)]
        acc = [ctx.enter_context(nc.psum_tensor(f"a_acc{i}", [P, CH], F32)) for i in range(BANKS)]

        w_loaded = [sem(f"w_loaded{k}") for k in range(KD)]
        w_hi_done = sem("w_hi_done")
        w_lo_done = sem("w_lo_done")
        const_done = sem("const_done")
        x_loaded = [sem(f"x_loaded{i}") for i in range(2)]
        stats_chain = sem("stats_chain")
        stats_seen = sem("stats_seen")
        stats_done = sem("stats_done")
        std_done = sem("std_done")
        rstd_done = sem("rstd_done")
        xn_done = sem("xn_done")
        turned = sem("turned")
        xt_hi_done = sem("xt_hi_done")
        xt_lo_done = sem("xt_lo_done")
        acc_done = sem("acc_done")
        qk_hi_done = sem("qk_hi_done")
        qk_lo_done = sem("qk_lo_done")
        v_done = sem("v_done")
        qk_stored = [sem(f"qk_stored{i}") for i in range(SLOTS)]
        v_stored = [sem(f"v_stored{i}") for i in range(2)]

        def rows(c):
            return bass.ds(c * CH, CH)

        with nc.Block() as block:
            @block.sync
            def _(sp):
                def load_x(i, p):
                    src = x[rows(2 * i + p), :].rearrange("(t p) d -> p t d", p=P)
                    sp.dma_start(x_in[:, p], src).then_inc(x_loaded[p], 16)

                def store(i, p):
                    c = 2 * i + p
                    for g in range(QKG):
                        dst = qk_dram[:, g // QUADS, :, g % QUADS, rows(c)].rearrange("s f t -> f s t")
                        sp.wait_ge(qk_lo_done, QKG * (c + 1) + g + 1)
                        sp.dma_start(dst, qk[:, g % SLOTS].bitcast(F32)).then_inc(qk_stored[g % SLOTS], 16)
                    sp.wait_ge(v_done, TILES * (c + 2))
                    for q in range(QUADS):
                        dst = v_dram[q, rows(c), :].rearrange("(t p) e -> p t e", p=P)
                        src = v[:, p, :, q * QH * E:(q + 1) * QH * E]
                        sp.dma_start(dst, src).then_inc(v_stored[p], 16)

                def chunk(i, p, more=True):
                    c = 2 * i + p
                    if more:
                        sp.wait_ge(xn_done, c + 1)
                        load_x(i + 1, p)
                    store(i, p)

                load_x(0, 0)
                for k in range(KD):
                    sp.dma_start(w_in[:, k, :], w_qkv[k * P:(k + 1) * P, :]).then_inc(w_loaded[k], 16)
                load_x(0, 1)
                with sp.Fori(0, PAIRS - 1) as i:
                    chunk(i, 0)
                    chunk(i, 1)
                chunk(PAIRS - 1, 0, more=False)
                chunk(PAIRS - 1, 1, more=False)
                for s in range(SLOTS):
                    sp.wait_ge(qk_stored[s], 16 * (1 + CHUNKS * QKG // SLOTS))
                for p in range(2):
                    sp.wait_ge(v_stored[p], 16 * QUADS * (1 + PAIRS))

            @block.gpsimd
            def _(pool):
                pool.memset(ident[:, :], 0.0).then_inc(const_done, 1)
                pool.memset(eps[:, :], EPS).then_inc(const_done, 1)
                pool.wait_ge(const_done, 2)
                pool.affine_select(out=ident[:, :], in_=ident[:, :], compare_op=ALU.not_equal, fill=1.0,
                                   base=0, pattern=[[-1, P]], channel_multiplier=1).then_inc(const_done, 1)
                for s in range(SLOTS):
                    pool.sem_inc(qk_stored[s], 16)
                for p in range(2):
                    pool.sem_inc(v_stored[p], 16 * QUADS)

            @block.scalar
            def _(act):
                act.sem_inc(v_done, TILES)
                act.wait_ge(const_done, 3)

                def take_sqrt(n):
                    act.wait_ge(stats_done, n)
                    act.activation(std[:, :], moments[:, :, 1], ACT.Sqrt, bias=eps[:, :]).then_inc(std_done, 1)

                def xt_block(c, p, k):
                    act.wait_ge(turned, KD * (c + 1) + k + 1)
                    act.activation(xt_hi[:, p, k, :], turn[k % 2][:, :], ACT.Copy).then_inc(xt_hi_done, 1)

                def qk_group(i, p, g):
                    c = 2 * i + p
                    act.wait_ge(qk_stored[g % SLOTS], 16 * (2 * c + g // SLOTS + 1))
                    act.wait_ge(acc_done, GROUPS * c + g + 1)
                    act.activation(qk[:, g % SLOTS, 0, :], acc[g % BANKS][:, :], ACT.Copy).then_inc(qk_hi_done, 1)

                def v_tile(i, p, t):
                    c = 2 * i + p
                    act.wait_ge(v_stored[p], 16 * QUADS * (i + 1))
                    act.wait_ge(acc_done, GROUPS * c + QKG + t + 1)
                    act.activation(v[:, p, t, :], acc[(QKG + t) % BANKS][:, :],
                                   ACT.Copy).then_inc(v_done, 1)

                def chunk(i, p, last=False):
                    c = 2 * i + p
                    if not last:
                        take_sqrt(c + 2)
                    for g in range(QKG):
                        qk_group(i, p, g)
                        if g >= QKG - KD and not last:
                            xt_block(c + 1, 1 - p, g - (QKG - KD))
                    for t in range(TILES):
                        v_tile(i, p, t)

                take_sqrt(1)
                for k in range(KD):
                    act.wait_ge(w_loaded[k], 16)
                    act.activation(w_hi[:, k, :], w_in[:, k, :], ACT.Copy).then_inc(w_hi_done, 1)
                for k in range(KD):
                    xt_block(0, 0, k)
                with act.Fori(0, PAIRS - 1) as i:
                    chunk(i, 0)
                    chunk(i, 1)
                chunk(PAIRS - 1, 0)
                chunk(PAIRS - 1, 1, last=True)

            @block.vector
            def _(dve):
                dve.sem_inc(qk_lo_done, QKG)
                dve.sem_inc(xt_lo_done, 2)

                def take_stats(i, p):
                    c = 2 * i + p
                    dve.wait_ge(x_loaded[p], 16 * (i + 1))
                    layernorm_stats(dve, x_in[:, p], stats, moments, stats_chain, stats_seen, TILES * c).then_inc(stats_done, 1)

                def normalise(i, p):
                    c = 2 * i + p
                    dve.wait_ge(std_done, c + 1)
                    dve.reciprocal(rstd[:, :], std[:, :]).then_inc(rstd_done, 1)
                    dve.wait_ge(rstd_done, c + 1)
                    for t in range(TILES):
                        last = dve.tensor_scalar(xn[:, p, t, :], x_in[:, p, t, :], moments[:, t, 0:1],
                                                 rstd[:, t:t + 1], ALU.subtract, ALU.mult)
                    last.then_inc(xn_done, 1)

                def xt_block(c, p, k):
                    dve.wait_ge(xt_hi_done, KD * c + k + 1)
                    dve.tensor_tensor(xt_lo[:, p, k, :], turn[k % 2][:, :], xt_hi[:, p, k, :],
                                      ALU.subtract).then_inc(xt_lo_done, 1)

                def qk_group(c, g):
                    dve.wait_ge(qk_hi_done, QKG * c + g + 1)
                    dve.tensor_tensor(qk[:, g % SLOTS, 1, :], acc[g % BANKS][:, :], qk[:, g % SLOTS, 0, :],
                                      ALU.subtract).then_inc(qk_lo_done, 1)

                def chunk(i, p, last=False):
                    c = 2 * i + p
                    if not last:
                        take_stats(i + p, 1 - p)
                    qk_group(c, 0)
                    if not last:
                        normalise(i + p, 1 - p)
                    for g in range(1, QKG):
                        qk_group(c, g)
                        if g >= QKG - KD and not last:
                            xt_block(c + 1, 1 - p, g - (QKG - KD))

                take_stats(0, 0)
                normalise(0, 0)
                for k in range(KD):
                    dve.wait_ge(w_hi_done, k + 1)
                    dve.tensor_tensor(w_lo[:, k, :], w_in[:, k, :], w_hi[:, k, :], ALU.subtract).then_inc(w_lo_done, 1)
                for k in range(KD):
                    xt_block(0, 0, k)
                with dve.Fori(0, PAIRS - 1) as i:
                    chunk(i, 0)
                    chunk(i, 1)
                chunk(PAIRS - 1, 0)
                chunk(PAIRS - 1, 1, last=True)

            @block.tensor
            def _(pe):
                pe.sem_inc(turned, KD)
                pe.wait_ge(const_done, 3)

                def turn_block(c, p, k):
                    pe.wait_ge(xn_done, c + 1)
                    pe.wait_ge(xt_lo_done, KD * c + k + 1)
                    for t in range(TILES):
                        mm = pe.transpose(turn[k % 2][:, t * P:(t + 1) * P], xn[:, p, t, k * P:(k + 1) * P], ident[:, :])
                    mm.then_inc(turned, 1)

                def product(out, terms):
                    for n, (lhs, rhs) in enumerate(terms):
                        mm = pe.matmul(out, lhs, rhs, start=(n == 0), stop=(n == len(terms) - 1))
                    return mm

                def group(c, p, g):
                    if g < BANKS:
                        prev = g + GROUPS - BANKS
                        if prev < QKG:
                            pe.wait_ge(qk_lo_done, QKG * c + prev + 1)
                        else:
                            pe.wait_ge(v_done, TILES * c + prev - QKG + 1)
                    else:
                        pe.wait_ge(qk_lo_done, QKG * (c + 1) + g - BANKS + 1)
                    if g == 0:
                        pe.wait_ge(xt_hi_done, KD * (c + 1))
                        pe.wait_ge(xt_lo_done, KD * (c + 1) + 2)
                    terms = []
                    for k in range(KD):
                        if g < QKG:
                            hi, lo = (w[:, k, g * P:(g + 1) * P] for w in (w_hi, w_lo))
                            th, tl = (t[:, p, k, :] for t in (xt_hi, xt_lo))
                            terms += [(hi, th), (hi, tl), (lo, th)]
                        else:
                            t = g - QKG
                            hi, lo = (w[:, k, 2 * D:3 * D] for w in (w_hi, w_lo))
                            th, tl = (x[:, p, k, t * P:(t + 1) * P] for x in (xt_hi, xt_lo))
                            terms += [(th, hi), (th, lo), (tl, hi)]
                    product(acc[g % BANKS][:, :], terms).then_inc(acc_done, 1)

                def chunk(i, p, last=False):
                    c = 2 * i + p
                    for g in range(GROUPS):
                        group(c, p, g)
                        if QKG - KD <= g < QKG and not last:
                            turn_block(c + 1, 1 - p, g - (QKG - KD))

                for k in range(KD):
                    turn_block(0, 0, k)
                pe.wait_ge(w_lo_done, KD)
                with pe.Fori(0, PAIRS - 1) as i:
                    chunk(i, 0)
                    chunk(i, 1)
                chunk(PAIRS - 1, 0)
                chunk(PAIRS - 1, 1, last=True)


def phase_attention(nc, qk_dram, v_dram, o_dram, load_unit):
    W = SEQ // WIN
    ROUNDS = QUADS * BATCH
    STACK = 3 * E
    AHEAD, TURN_M, PV_LAG, OUT_LAG = 4, 3, 2, 3
    FIRST, LAST = -AHEAD, OUT_LAG
    RING = 4
    LOADS = 7
    with ExitStack() as ctx:
        def sb(name, shape, dt):
            return ctx.enter_context(nc.sbuf_tensor("b_" + name, shape, dt))

        def psum(name, shape):
            return ctx.enter_context(nc.psum_tensor("b_" + name, shape, F32))

        def sem(name):
            return nc.alloc_semaphore("b_" + name)

        q_st = sb("q_st", [P, QH, SEQ], F32R)
        k_st = sb("k_st", [P, QH, SEQ], F32R)
        v_sb = sb("v_sb", [P, W, QH * E], F32)
        ones = sb("ones", [P, E], F32)
        probs = sb("probs", [P, RING, QH, 3 * WIN], F32)
        neg_max = sb("neg_max", [P, 2, QH], F32)
        max_rows = sb("max_rows", [QH, RING, WIN], F32R)
        total = sb("total", [P, 2, QH, WIN], F32)
        ident = sb("ident", [P, P], F32)
        out_t = sb("out_t", [P, 2, 2, WIN], F32)
        inv_sum = sb("inv_sum", [P, 2, QH], F32)
        out = sb("out", [P, 2, 4, QH * E], F32)
        ps_score = psum("ps_score", [P, 2, 512])
        ps_keys = [psum(f"ps_keys{i}", [P, 2, 512]) for i in range(2)]
        ps_out = psum("ps_out", [P, 512])
        ps_turn = psum("ps_turn", [P, 512])

        const_done = sem("const_done")
        loaded = [sem(f"loaded{i}") for i in range(4)]
        scored = sem("scored")
        reduced = sem("reduced")
        max_turned = sem("max_turned")
        rows_done = sem("rows_done")
        rows_landed = [sem(f"rows_landed{i}") for i in range(RING)]
        keys_done = sem("keys_done")
        exp_done = sem("exp_done")
        pv_done = sem("pv_done")
        part_summed = sem("part_summed")
        summed = sem("summed")
        out_copied = sem("out_copied")
        out_turned = sem("out_turned")
        inv_done = sem("inv_done")
        out_done = sem("out_done")
        out_stored = [sem(f"out_stored{i}") for i in range(2)]

        def span(w):
            return max(w - 1, 0), min(w + 2, W)

        def steps(eng, step):
            for j in range(FIRST, LAST):
                step(0, j, lambda m: m >= 0)
            with eng.Fori(0, ROUNDS - 1) as n:
                for j in range(LAST, LAST + W):
                    step(n, j, lambda m: True)
            for j in range(LAST, LAST + W):
                step(ROUNDS - 1, j, lambda m: m < W)

        with nc.Block() as block:
            @block.sync
            def _(sp):
                for s in rows_landed:
                    sp.sem_inc(s, 16)

                def load(n, c, third=None):
                    if isinstance(n, int):
                        tokens = slice(n * SEQ + c * CH, n * SEQ + (c + 1) * CH)
                    else:
                        tokens = bass.ds(n * SEQ + c * CH, CH)
                    parts = [(q_st, 0, 0), (q_st, 0, 1), (q_st, 0, 0), (k_st, 1, 0), (k_st, 1, 0), (k_st, 1, 1)]
                    for part, (dst, which, half) in enumerate(parts):
                        if third not in (None, part // 2):
                            continue
                        r = part % 3
                        src = qk_dram[half, which].rearrange("f q t -> f (q t)")[:, tokens]
                        sp.dma_start(dst[r * E:(r + 1) * E, :, c * CH:(c + 1) * CH].bitcast(F32),
                                     src.rearrange("(h e) t -> e h t", e=E)).then_inc(loaded[c], 16)
                    if third in (None, 2):
                        src = v_dram.rearrange("q t e -> (q t) e")[tokens, :].rearrange("(w p) e -> p w e", p=P)
                        sp.dma_start(v_sb[:, c * 4:(c + 1) * 4, :], src).then_inc(loaded[c], 16)

                def store(n, c):
                    tokens = bass.ds(n * SEQ + c * CH, CH)
                    dst = o_dram.rearrange("q t e -> (q t) e")[tokens, :].rearrange("(w p) e -> p w e", p=P)
                    sp.wait_ge(out_done, 8 + W * n + 4 * c + 4)
                    sp.dma_start(dst, out[:, c % 2]).then_inc(out_stored[c % 2], 16)

                def step(n, j, there):
                    if there(j + TURN_M):
                        g = j + TURN_M
                        sp.wait_ge(rows_done, W * n + g + 1)
                        w = g % W
                        sp.dma_start(q_st[STACK:STACK + 1, :, w * WIN:(w + 1) * WIN].bitcast(F32),
                                     max_rows[:, g % RING, :].bitcast(F32)).then_inc(rows_landed[g % RING], 16)
                    if 3 <= j < 6:
                        if j == 3:
                            sp.wait_ge(pv_done, 4 + W * n)
                        load(n, 3, j - 3)
                    for c in range(3):
                        if 7 + 4 * c <= j < 10 + 4 * c and not there(W):
                            load_unit(sp, 3 * c + j - 7 - 4 * c)
                        elif 7 + 4 * c <= j < 10 + 4 * c:
                            if j == 7 + 4 * c:
                                sp.wait_ge(pv_done, 4 + W * n + 4 * c + 5)
                            load(n + 1, c, j - 7 - 4 * c)
                        if j == 7 + 4 * c:
                            store(n, c)

                for c in range(3):
                    load(0, c)
                for j in range(FIRST, LAST):
                    step(0, j, lambda m: m >= 0)
                with sp.Fori(0, ROUNDS - 1) as n:
                    for j in range(LAST, LAST + W):
                        step(n, j, lambda m: True)
                    store(n, 3)
                for j in range(LAST, LAST + W):
                    step(ROUNDS - 1, j, lambda m: m < W)
                store(ROUNDS - 1, 3)
                for s in out_stored:
                    sp.wait_ge(s, 16 * (1 + 2 * ROUNDS))

            @block.gpsimd
            def _(pool):
                pool.memset(ident[:, :], 0.0).then_inc(const_done, 1)
                pool.wait_ge(const_done, 1)
                pool.affine_select(out=ident[:, :], in_=ident[:, :], compare_op=ALU.not_equal, fill=1.0,
                                   base=0, pattern=[[-1, P]], channel_multiplier=1).then_inc(const_done, 1)
                pool.wait_ge(const_done, 2)
                pool.memset(ones[:, :], 1.0).then_inc(const_done, 1)
                pool.wait_ge(const_done, 3)
                pool.memset(k_st[STACK:STACK + 1, :, :].bitcast(F32), 1.0).then_inc(const_done, 1)
                for s in out_stored:
                    pool.sem_inc(s, 16)

                def sum_weights(n, m):
                    w = m % W
                    lo, hi = span(w)
                    parts = [probs[:, kb % RING, :, (w - span(kb)[0]) * WIN:(w - span(kb)[0] + 1) * WIN]
                             for kb in range(lo, hi)]
                    pool.wait_ge(exp_done, 2 + 2 * (W * n + m - w + lo + 2))
                    pool.wait_ge(pv_done, W * n + m + 3)
                    first = pool.tensor_tensor(total[:, m % 2], parts[0], parts[1], ALU.add)
                    first.then_inc(part_summed if len(parts) > 2 else summed, 1)
                    if len(parts) > 2:
                        pool.wait_ge(exp_done, 2 + 2 * (W * n + m - w + hi))
                        pool.wait_ge(part_summed, (W - 2) * (n + m // W) + w)
                        pool.tensor_tensor(total[:, m % 2], total[:, m % 2], parts[2], ALU.add).then_inc(summed, 1)

                def step(n, j, there):
                    if there(j - PV_LAG):
                        sum_weights(n, j - PV_LAG)

                steps(pool, step)

            @block.tensor
            def _(pe):
                pe.sem_inc(pv_done, 4)
                pe.sem_inc(max_turned, 2)
                pe.wait_ge(const_done, 4)

                def score(n, m, h):
                    w = m % W
                    lo, hi = span(w)
                    if h == 0 and w in (0, 3, 7, 11):
                        pe.wait_ge(loaded[(w + 1) // 4], 16 * LOADS * (n + m // W + 1))
                    pe.wait_ge(reduced, QH * (W * n + m) + h + 1)
                    mm = pe.matmul(ps_score[:, h % 2, 0:(hi - lo) * WIN], q_st[0:STACK, h, w * WIN:(w + 1) * WIN],
                                   k_st[0:STACK, h, lo * WIN:hi * WIN], start=True, stop=True)
                    mm.then_inc(scored, 1)

                def keys(n, m, pair):
                    w = m % W
                    lo, hi = span(w)
                    if pair == 0:
                        for u in ([w] if w == 0 else []) + ([w + 1] if w + 1 < W else []):
                            g = m - w + u
                            pe.wait_ge(rows_landed[g % RING], 16 * (W // RING * n + g // RING + 2))
                    pe.wait_ge(exp_done, 2 * (W * n + m) + pair + 1)
                    for i in range(2):
                        h = 2 * pair + i
                        mm = pe.matmul(ps_keys[pair][:, i, 0:(hi - lo) * WIN], k_st[0:STACK + 1, h, w * WIN:(w + 1) * WIN],
                                       q_st[0:STACK + 1, h, lo * WIN:hi * WIN], start=True, stop=True)
                    mm.then_inc(keys_done, 1)

                def turn_max(n, m):
                    pe.wait_ge(out_done, 8 + W * n + m - TURN_M - OUT_LAG)
                    pe.wait_ge(reduced, QH * (W * n + m + 1) + 2)
                    pe.transpose(ps_turn[0:QH, 0:P], neg_max[:, m % 2, :], ident[:, :]).then_inc(max_turned, 1)

                def values(n, m):
                    w = m % W
                    lo, hi = span(w)
                    pe.wait_ge(exp_done, 2 + 2 * (W * n + m - w + hi))
                    pe.wait_ge(out_copied, W * n + m + 1)
                    for kb in range(lo, hi):
                        col = (w - span(kb)[0]) * WIN
                        for h in range(QH):
                            pe.matmul(ps_out[h * E:(h + 1) * E, 0:WIN], v_sb[:, kb, h * E:(h + 1) * E],
                                      probs[:, kb % RING, h, col:col + WIN],
                                      start=(kb == lo), stop=(kb == hi - 1), skip_group_check=True)

                def sums(n, m):
                    pe.wait_ge(summed, W * n + m + 1)
                    for h in range(QH):
                        mm = pe.matmul(ps_out[h * E:(h + 1) * E, WIN:2 * WIN], ones[:, :], total[:, m % 2, h, :],
                                       start=True, stop=True, skip_group_check=True)
                    mm.then_inc(pv_done, 1)

                def turn_out(n, m, after_max):
                    if after_max:
                        pe.wait_ge(rows_done, W * n + m + OUT_LAG + TURN_M + 1)
                    else:
                        pe.wait_ge(out_done, 8 + W * n + m)
                    pe.wait_ge(out_copied, 2 + W * n + m)
                    for part in range(2):
                        mm = pe.transpose(ps_turn[:, part * P:(part + 1) * P], out_t[:, m % 2, part, :], ident[:, :])
                    mm.then_inc(out_turned, 1)

                def step(n, j, there):
                    if there(j):
                        keys(n, j, 0)
                    if there(j + AHEAD):
                        score(n, j + AHEAD, 0)
                    if there(j):
                        keys(n, j, 1)
                    if there(j + AHEAD):
                        score(n, j + AHEAD, 1)
                    if there(j + TURN_M):
                        turn_max(n, j + TURN_M)
                    if there(j - PV_LAG):
                        values(n, j - PV_LAG)
                    if there(j + AHEAD):
                        score(n, j + AHEAD, 2)
                    if there(j - OUT_LAG):
                        turn_out(n, j - OUT_LAG, there(j + TURN_M))
                    if there(j + AHEAD):
                        score(n, j + AHEAD, 3)
                    if there(j - PV_LAG):
                        sums(n, j - PV_LAG)

                steps(pe, step)

            @block.scalar
            def _(act):
                act.sem_inc(exp_done, 2)
                act.sem_inc(out_copied, 1)

                def weights(n, m, pair):
                    w = m % W
                    lo, hi = span(w)
                    if pair == 0:
                        act.wait_ge(pv_done, W * n + m + 2)
                    act.wait_ge(keys_done, 2 * (W * n + m) + pair + 1)
                    act.activation(probs[:, w % RING, 2 * pair:2 * pair + 2, 0:(hi - lo) * WIN],
                                   ps_keys[pair][:, :, 0:(hi - lo) * WIN], ACT.Exp, scale=SCALE).then_inc(exp_done, 1)

                def copy_out(n, m):
                    act.wait_ge(pv_done, 4 + W * n + m + 1)
                    act.activation(out_t[:, m % 2].rearrange("p a q -> p (a q)"), ps_out[:, 0:2 * WIN],
                                   ACT.Copy).then_inc(out_copied, 1)

                def step(n, j, there):
                    for pair in range(2):
                        if there(j):
                            weights(n, j, pair)
                    if there(j - PV_LAG):
                        copy_out(n, j - PV_LAG)

                steps(act, step)

            @block.vector
            def _(dve):
                dve.sem_inc(reduced, 2)
                dve.sem_inc(out_done, 8)

                def reduce(n, m, h):
                    w = m % W
                    lo, hi = span(w)
                    if h == 0:
                        dve.wait_ge(max_turned, W * n + m + 1)
                    dve.wait_ge(scored, QH * (W * n + m) + h + 1)
                    dve.tensor_reduce(neg_max[:, m % 2, h:h + 1], ps_score[:, h % 2, 0:(hi - lo) * WIN],
                                      AX_X, ALU.max, negate=True).then_inc(reduced, 1)

                def copy_rows(n, m):
                    dve.wait_ge(rows_landed[m % RING], 16 * (W // RING * n + m // RING + 1))
                    dve.wait_ge(max_turned, 2 + W * n + m + 1)
                    dve.tensor_copy(max_rows[:, m % RING, :], ps_turn[0:QH, 0:P]).then_inc(rows_done, 1)

                def normalise(n, m):
                    w = m % W
                    dve.wait_ge(out_turned, W * n + m + 1)
                    sums = ps_turn[:, P:2 * P].rearrange("p (h e) -> p h e", h=QH)[:, :, 0]
                    dve.reciprocal(inv_sum[:, m % 2, :], sums).then_inc(inv_done, 1)
                    dve.wait_ge(inv_done, W * n + m + 1)
                    if w % 4 == 0:
                        dve.wait_ge(out_stored[w // 4 % 2], 16 * (2 * (n + m // W) + w // 8 + 1))
                    dve.tensor_tensor(out[:, w // 4 % 2, w % 4, :].rearrange("p (h e) -> p h e", h=QH),
                                      ps_turn[:, 0:P].rearrange("p (h e) -> p h e", h=QH),
                                      inv_sum[:, m % 2, :].unsqueeze(2).to_broadcast([P, QH, E]),
                                      ALU.mult).then_inc(out_done, 1)

                def step(n, j, there):
                    for h in range(QH):
                        if there(j + AHEAD):
                            reduce(n, j + AHEAD, h)
                        if h == 1 and there(j + TURN_M):
                            copy_rows(n, j + TURN_M)
                    if there(j - OUT_LAG):
                        normalise(n, j - OUT_LAG)

                steps(dve, step)


def phase_gate(nc, x, gate_w1, gate_b1, o_dram, x1_dram, yt_dram, gate_sum):
    KD = D // P
    PAIRS = CHUNKS // 2
    LOADS = QUADS + 1
    with ExitStack() as ctx:
        def sb(name, shape, dt):
            return ctx.enter_context(nc.sbuf_tensor("c_" + name, shape, dt))

        def sem(name):
            return nc.alloc_semaphore("c_" + name)

        w_hi = sb("w_hi", [P, KD, D], F32R)
        w_lo = sb("w_lo", [P, KD, D], F32R)
        b1 = sb("b1", [P, KD], F32)
        ident = sb("ident", [P, P], F32)
        eps = sb("eps", [P, 1], F32)
        att = sb("att", [P, 2, TILES, D], F32)
        x_in = sb("x_in", [P, 2, TILES, D], F32)
        x1 = sb("x1", [P, 2, TILES, D], F32)
        y = sb("y", [P, 2, TILES, D], F32)
        yt = sb("yt", [P, 2, KD, CH], F32)
        w_in = yt[:, 1]
        yt_hi = sb("yt_hi", [P, 2, KD, CH], F32R)
        yt_lo = sb("yt_lo", [P, 2, KD, CH], F32R)
        stats = sb("stats", [P, 2, TILES, 6], F32)
        moments = sb("moments", [P, 2, TILES, 2], F32)
        std = sb("std", [P, 2, TILES], F32)
        rstd = sb("rstd", [P, 2, TILES], F32)
        shift = sb("shift", [P, TILES], F32)
        turn = [ctx.enter_context(nc.psum_tensor(f"c_turn{i}", [P, CH], F32)) for i in range(KD)]
        acc = [ctx.enter_context(nc.psum_tensor(f"c_acc{i}", [P, CH], F32)) for i in range(KD)]

        w_loaded = sem("w_loaded")
        w_hi_done = sem("w_hi_done")
        w_lo_done = sem("w_lo_done")
        const_done = sem("const_done")
        loaded = [sem(f"loaded{i}") for i in range(2)]
        chain = [sem(f"chain{i}") for i in range(2)]
        stats_seen = sem("stats_seen")
        stats_done = [sem(f"stats_done{i}") for i in range(2)]
        std_done = [sem(f"std_done{i}") for i in range(2)]
        rstd_done = [sem(f"rstd_done{i}") for i in range(2)]
        shift_done = sem("shift_done")
        att_done = sem("att_done")
        x1_done = sem("x1_done")
        y_done = sem("y_done")
        turned = sem("turned")
        hi_done = sem("hi_done")
        lo_done = sem("lo_done")
        yt_done = sem("yt_done")
        yt_seen = sem("yt_seen")
        gate_done = sem("gate_done")
        relu_done = sem("relu_done")
        x1_stored = [sem(f"x1_stored{i}") for i in range(2)]
        yt_stored = [sem(f"yt_stored{i}") for i in range(2)]

        def ahead(i, p, d):
            return 2 * i + p + d, (p + d) % 2, i + (p + d) // 2

        def steps(eng, step):
            step(-2, 1, lambda d: d == 3)
            step(-1, 0, lambda d: d >= 2)
            step(-1, 1, lambda d: d >= 1)
            with eng.Fori(0, PAIRS - 2) as i:
                step(i, 0, lambda d: True)
                step(i, 1, lambda d: True)
            step(PAIRS - 2, 0, lambda d: True)
            step(PAIRS - 2, 1, lambda d: d < 3)
            step(PAIRS - 1, 0, lambda d: d < 2)
            step(PAIRS - 1, 1, lambda d: d < 1)

        with nc.Block() as block:
            @block.sync
            def _(sp):
                for p in range(2):
                    sp.sem_inc(x1_stored[p], 16)
                    sp.sem_inc(yt_stored[p], 16)

                def load(c, p):
                    rows = slice(c * CH, (c + 1) * CH) if isinstance(c, int) else bass.ds(c * CH, CH)
                    for q in range(QUADS):
                        sp.dma_start(att[:, p, :, q * P:(q + 1) * P],
                                     o_dram[q, rows, :].rearrange("(t p) e -> p t e", p=P)).then_inc(loaded[p], 16)
                    sp.dma_start(x_in[:, p], x[rows, :].rearrange("(t p) d -> p t d", p=P)).then_inc(loaded[p], 16)

                def store_x1(i, p):
                    c, p, _ = ahead(i, p, 3)
                    rows = bass.ds(CH * c, CH)
                    sp.wait_ge(x1_done, TILES * (c + 1))
                    sp.dma_start(x1_dram[rows, :].rearrange("(t p) d -> p t d", p=P), x1[:, p]).then_inc(x1_stored[p], 16)

                def store_yt(i, p):
                    c, p, _ = ahead(i, p, 1)
                    cols = bass.ds(CH * c, CH)
                    sp.wait_ge(yt_done, KD * (c + 3))
                    sp.sem_inc(yt_seen, 1)
                    sp.dma_start(yt_dram[:, cols].rearrange("(k p) t -> p k t", p=P), yt[:, p]).then_inc(yt_stored[p], 16)

                def step(i, p, has, more=True):
                    if has(3):
                        c = 2 * i + p
                        store_x1(i, p)
                        if more:
                            load(c + 5, (p + 5) % 2)
                    if has(1):
                        store_yt(i, p)

                load(0, 0)
                sp.dma_start(w_in, gate_w1.rearrange("(k p) n -> p k n", p=P)).then_inc(w_loaded, 16)
                sp.dma_start(b1[:, :], gate_b1).then_inc(w_loaded, 16)
                load(1, 1)
                step(-2, 1, lambda d: d == 3)
                step(-1, 0, lambda d: d >= 2)
                step(-1, 1, lambda d: d >= 1)
                with sp.Fori(0, PAIRS - 3) as i:
                    step(i, 0, lambda d: True)
                    step(i, 1, lambda d: True)
                step(PAIRS - 3, 0, lambda d: True)
                step(PAIRS - 3, 1, lambda d: True, more=False)
                step(PAIRS - 2, 0, lambda d: True, more=False)
                step(PAIRS - 2, 1, lambda d: d < 3)
                step(PAIRS - 1, 0, lambda d: d < 2)
                step(PAIRS - 1, 1, lambda d: d < 1)
                for p in range(2):
                    sp.wait_ge(x1_stored[p], 16 * (1 + PAIRS))
                    sp.wait_ge(yt_stored[p], 16 * (1 + PAIRS))

            @block.gpsimd
            def _(pool):
                pool.memset(ident[:, :], 0.0).then_inc(const_done, 1)
                pool.memset(eps[:, :], EPS).then_inc(const_done, 1)
                pool.wait_ge(const_done, 2)
                pool.affine_select(out=ident[:, :], in_=ident[:, :], compare_op=ALU.not_equal, fill=1.0,
                                   base=0, pattern=[[-1, P]], channel_multiplier=1).then_inc(const_done, 1)

                def add_x(i, p):
                    c, p, _ = ahead(i, p, 3)
                    for t in range(TILES):
                        pool.wait_ge(att_done, TILES * c + t + 1)
                        pool.tensor_tensor(x1[:, p, t, :], x1[:, p, t, :], x_in[:, p, t, :], ALU.add).then_inc(x1_done, 1)

                def add_halves(i, p):
                    c, p, before = ahead(i, p, 1)
                    pool.wait_ge(yt_stored[p], 16 * (before + 1))
                    for k in range(KD):
                        pool.wait_ge(lo_done, KD * (c + 1) + k + 1)
                        pool.tensor_tensor(yt[:, p, k, :], yt_hi[:, p, k, :], yt_lo[:, p, k, :], ALU.add).then_inc(yt_done, 1)

                def step(i, p, has):
                    if has(3):
                        add_x(i, p)
                    if has(1):
                        add_halves(i, p)

                steps(pool, step)

            @block.scalar
            def _(act):
                act.sem_inc(relu_done, KD)
                act.sem_inc(yt_done, 2 * KD)
                act.wait_ge(const_done, 3)

                def take_sqrt(c, which):
                    act.wait_ge(stats_done[which], c + 1)
                    act.activation(std[:, which, :], moments[:, which, :, 1], ACT.Sqrt,
                                   bias=eps[:, :]).then_inc(std_done[which], 1)

                def attention_tiles(i, p):
                    c, p, before = ahead(i, p, 3)
                    act.wait_ge(shift_done, c + 1)
                    act.wait_ge(x1_stored[p], 16 * (before + 1))
                    for t in range(TILES):
                        act.activation(x1[:, p, t, :], att[:, p, t, :], ACT.Identity, bias=shift[:, t:t + 1],
                                       scale=rstd[:, 0, t:t + 1]).then_inc(att_done, 1)

                def high(i, p, k):
                    c, p, _ = ahead(i, p, 1)
                    if k == 0:
                        act.wait_ge(yt_done, KD * (c + 1))
                    act.wait_ge(turned, KD * c + k + 1)
                    act.activation(yt_hi[:, p, k, :], turn[k][:, :], ACT.Copy).then_inc(hi_done, 1)

                def relu(c, m):
                    act.wait_ge(gate_done, KD * c + m + 1)
                    act.activation(acc[m][:, :], acc[m][:, :], ACT.Relu, bias=b1[:, m:m + 1],
                                   accum_out=gate_sum[:, m, bass.ds(c, 1)]).then_inc(relu_done, 1)

                def step(i, p, has):
                    c = 2 * i + p
                    if has(3):
                        take_sqrt(c + 3, 0)
                    if has(0):
                        relu(c, 0)
                    if has(1):
                        for k in range(KD):
                            high(i, p, k)
                    if has(3):
                        attention_tiles(i, p)
                    if has(0):
                        relu(c, 1)
                    if has(2):
                        take_sqrt(c + 2, 1)
                    if has(0):
                        for m in range(2, KD):
                            relu(c, m)
                    if isinstance(i, int) and i == -1 and p == 0:
                        split_weights()

                def split_weights():
                    act.wait_ge(w_loaded, 32)
                    for k in range(KD):
                        act.activation(w_hi[:, k, :], w_in[:, k, :], ACT.Copy).then_inc(w_hi_done, 1)

                steps(act, step)

            @block.vector
            def _(dve):
                dve.sem_inc(lo_done, KD)

                def take_stats(i, p, which):
                    c, p, before = ahead(i, p, 3 - which)
                    if which == 0:
                        dve.wait_ge(loaded[p], 16 * LOADS * (before + 1))
                        rows = att[:, p]
                    else:
                        dve.wait_ge(x1_done, TILES * (c + 1))
                        rows = x1[:, p]
                    for t in range(TILES):
                        dve.bn_stats(stats[:, which, t, :], rows[:, t, :]).then_inc(chain[which], 1)
                    dve.wait_ge(chain[which], TILES * (c + 1))
                    dve.sem_inc(stats_seen, 1)
                    for t in range(TILES):
                        last = dve.bn_aggr(moments[:, which, t, :], stats[:, which, t, :])
                    last.then_inc(stats_done[which], 1)

                def invert(i, p, which):
                    c, _, _ = ahead(i, p, 3 - which)
                    dve.wait_ge(std_done[which], c + 1)
                    dve.reciprocal(rstd[:, which, :], std[:, which, :]).then_inc(rstd_done[which], 1)
                    dve.wait_ge(rstd_done[which], c + 1)

                def low(i, p, k):
                    c, p, _ = ahead(i, p, 1)
                    dve.wait_ge(hi_done, KD * c + k + 1)
                    dve.tensor_tensor(yt_lo[:, p, k, :], turn[k][:, :], yt_hi[:, p, k, :],
                                      ALU.subtract).then_inc(lo_done, 1)

                def make_shift():
                    dve.scalar_tensor_tensor(out=shift[:, :], in0=moments[:, 0, :, 0], scalar=-1.0, in1=rstd[:, 0, :],
                                             op0=ALU.mult, op1=ALU.mult).then_inc(shift_done, 1)

                def make_y(i, p):
                    c, p, _ = ahead(i, p, 2)
                    dve.wait_ge(turned, KD * c)
                    for t in range(TILES):
                        last = dve.tensor_scalar(y[:, p, t, :], x1[:, p, t, :], moments[:, 1, t, 0:1],
                                                 rstd[:, 1, t:t + 1], ALU.subtract, ALU.mult)
                    last.then_inc(y_done, 1)

                def step(i, p, has):
                    if has(3):
                        take_stats(i, p, 0)
                        invert(i, p, 0)
                        make_shift()
                    if has(1):
                        for k in range(KD):
                            low(i, p, k)
                    if has(2):
                        take_stats(i, p, 1)
                        invert(i, p, 1)
                        make_y(i, p)
                    if isinstance(i, int) and i == -1 and p == 0:
                        split_weights()

                def split_weights():
                    for k in range(KD):
                        dve.wait_ge(w_hi_done, k + 1)
                        dve.tensor_tensor(w_lo[:, k, :], w_in[:, k, :], w_hi[:, k, :], ALU.subtract).then_inc(w_lo_done, 1)

                steps(dve, step)

            @block.tensor
            def _(pe):
                pe.wait_ge(const_done, 3)

                def turn_block(i, p, k):
                    c, p, _ = ahead(i, p, 1)
                    if k == 0:
                        pe.wait_ge(y_done, c + 1)
                    pe.wait_ge(lo_done, KD * c + k + 1)
                    for t in range(TILES):
                        mm = pe.transpose(turn[k][:, t * P:(t + 1) * P], y[:, p, t, k * P:(k + 1) * P], ident[:, :])
                    mm.then_inc(turned, 1)

                def gate(c, p, m):
                    if m == 0:
                        pe.wait_ge(w_lo_done, KD)
                    pe.wait_ge(relu_done, KD * c + m + 1)
                    cols = slice(m * P, (m + 1) * P)
                    for k in range(KD):
                        if m == 0:
                            pe.wait_ge(lo_done, KD * (c + 1) + k + 1)
                        pe.matmul(acc[m][:, :], w_hi[:, k, cols], yt_hi[:, p, k, :], start=(k == 0), stop=False)
                        pe.matmul(acc[m][:, :], w_hi[:, k, cols], yt_lo[:, p, k, :], start=False, stop=False)
                        mm = pe.matmul(acc[m][:, :], w_lo[:, k, cols], yt_hi[:, p, k, :], start=False, stop=(k == KD - 1))
                    mm.then_inc(gate_done, 1)

                def step(i, p, has):
                    c = 2 * i + p
                    if has(0):
                        gate(c, p, 0)
                    if has(1):
                        for k in range(KD):
                            turn_block(i, p, k)
                    if has(0):
                        for m in range(1, KD):
                            gate(c, p, m)

                steps(pe, step)


def unit_loader(experts, units, unit_loaded):
    def load_unit(sp, n):
        if n < 2 * len(unit_loaded):
            sp.dma_start(units[:, n // 2, n % 2, :], experts[n]).then_inc(unit_loaded[n // 2], 16)
    return load_unit


def phase_mix(nc, mask_rows, pick_rows, base, experts, gate_w2, gate_b2_rows, gate_b2, b1, b2, tb1, tb2, gate_sum,
              units, unit_loaded, mix_dram, mb1, mb2):
    KD = D // P
    EX = EXPERTS
    R = P // EX
    M = BATCH * R
    COLS = FF
    UNITS = experts.shape[0]
    PAIRS = UNITS // 2
    RING = len(unit_loaded)
    with ExitStack() as ctx:
        def sb(name, shape, dt):
            return ctx.enter_context(nc.sbuf_tensor("d_" + name, shape, dt))

        def sem(name):
            return nc.alloc_semaphore("d_" + name)

        w2 = sb("w2", [P, KD, EX], F32)
        w2_wide = sb("w2_wide", [P, KD, EX, R], F32)
        bias_rows = sb("bias_rows", [P, 1], F32)
        bias = sb("bias", [EX, 1], F32)
        mask = sb("mask", [P, R], F32)
        b_sum = sb("b_sum", [P, KD, BATCH], F32)
        g_rows = sb("g_rows", [P, BATCH], F32)
        g = sb("g", [EX, BATCH], F32)
        g_wide = sb("g_wide", [EX, BATCH, P], F32)
        g_blocks = sb("g_blocks", [P, BATCH, R], F32)
        tb1_sb = sb("tb1", [EX, FF], F32)
        tb2_sb = sb("tb2", [EX, D], F32)
        b1_sb = sb("b1", [P, FF // P], F32)
        b2_sb = sb("b2", [P, D], F32)
        pick_in = sb("pick_in", [4 * R, 2 * M], F32)
        pick = sb("pick", [4 * R, 2 * M], F32R)
        base_rows = sb("base_rows", [2 * R, RING, COLS], F32)
        base_parts = sb("base_parts", [4 * R, 2, COLS], F32R)
        mixed = sb("mixed", [P, 2, COLS], F32)
        bank = [ctx.enter_context(nc.psum_tensor(f"d_bank{i}", [P, 2, 512], F32)) for i in range(4)]

        small_loaded = sem("small_loaded")
        wide_done = sem("wide_done")
        sum_done = sem("sum_done")
        g_psum = sem("g_psum")
        g_rows_done = sem("g_rows_done")
        g_done = sem("g_done")
        g_wide_done = sem("g_wide_done")
        g_blocks_done = sem("g_blocks_done")
        bias_psum = sem("bias_psum")
        bias_done = sem("bias_done")
        base_hi_done = sem("base_hi_done")
        base_lo_done = sem("base_lo_done")
        parts_used = sem("parts_used")
        mix_done = sem("mix_done")
        act_done = sem("act_done")
        dve_done = sem("dve_done")
        stored = [sem(f"stored{i}") for i in range(2)]

        with nc.Block() as block:
            @block.sync
            def _(sp):
                def load(i, slot, with_units=True):
                    rows = bass.ds(i, 1)
                    for u in range(2 if with_units else 0):
                        sp.dma_start(units[:, slot, u, :],
                                     experts.rearrange("(i u) p n -> i u p n", u=2)[rows, u].rearrange("i p n -> (i p) n")
                                     ).then_inc(unit_loaded[slot], 16)
                    sp.dma_start(base_rows[:, slot, :], base.rearrange("(i r) n -> i r n", r=2 * R)[rows].rearrange("i r n -> (i r) n")
                                 ).then_inc(unit_loaded[slot], 16)

                for dst, src in ((w2[:, :, :], gate_w2.rearrange("(k p) e -> p k e", p=P)), (bias_rows[:, :], gate_b2_rows),
                                 (bias[:, :], gate_b2), (mask[:, :], mask_rows), (pick_in[:, :], pick_rows), (tb1_sb[:, :], tb1), (tb2_sb[:, :], tb2),
                                 (b1_sb[:, :], b1), (b2_sb[:, :], b2)):
                    sp.dma_start(dst, src).then_inc(small_loaded, 16)
                for s in range(RING):
                    load(s, s, with_units=False)

                def pair(it, s, more=True):
                    i = RING * it + s
                    if more:
                        sp.wait_ge(mix_done, 4 * (i + 1))
                        load(i + RING, s)
                    sp.wait_ge(act_done, 2 * (i + 1) + 2)
                    sp.wait_ge(dve_done, 2 * (i + 1) + 2)
                    for u in range(2):
                        for b in range(BATCH):
                            row = (2 * i + u) * R
                            sp.dma_start(mix_dram[b, bass.ds(row, R), :],
                                         mixed[u * M + b * R:u * M + (b + 1) * R, s % 2, :]).then_inc(stored[s % 2], 16)

                with sp.Fori(0, PAIRS // RING - 1) as it:
                    for s in range(RING):
                        pair(it, s)
                for s in range(RING):
                    pair(PAIRS // RING - 1, s, more=False)
                for s in stored:
                    sp.wait_ge(s, 16 * 2 * BATCH * (1 + PAIRS // 2))

            @block.tensor
            def _(pe):
                pe.sem_inc(parts_used, 2)
                pe.wait_ge(wide_done, 1)
                pe.wait_ge(sum_done, 1)
                pe.wait_ge(small_loaded, 16 * 9)
                for k in range(KD):
                    pe.matmul(bank[0][:, 0, 0:BATCH], w2_wide[:, k].rearrange("p e r -> p (e r)"), b_sum[:, k, :],
                              start=(k == 0), stop=(k == KD - 1))
                for k in range(KD):
                    mm = pe.matmul(bank[0][0:EX, 1, 0:BATCH], w2[:, k, :], b_sum[:, k, :], start=(k == 0), stop=(k == KD - 1))
                mm.then_inc(g_psum, 1)
                pe.wait_ge(g_blocks_done, 1)

                def biases():
                    pe.wait_ge(g_wide_done, BATCH)
                    for j in range(FF // P):
                        mm = pe.matmul(bank[0][:, 1, BATCH * j:BATCH * (j + 1)], tb1_sb[:, j * P:(j + 1) * P], g[:, :],
                                       start=True, stop=True)
                    mm.then_inc(bias_psum, 1)
                    for b in range(BATCH):
                        if b == BATCH - 1:
                            pe.wait_ge(bias_done, 1)
                        mm = pe.matmul(bank[(b + 1) % 4][:, 1, :], g_wide[:, b, :], tb2_sb[:, :], start=True, stop=True)
                        mm.then_inc(bias_psum, 1)

                def pair(it, s):
                    i = RING * it + s
                    pe.wait_ge(base_lo_done, i + 1)
                    for q in range(4):
                        if q == 0:
                            pe.wait_ge(unit_loaded[s], 48 * (it + 1))
                        if q < 2:
                            pe.wait_ge(act_done, 2 * i + q + 1)
                        else:
                            pe.wait_ge(dve_done, 2 * i + q - 1)
                        mm = pe.matmul(bank[q][:, 0, :], pick[:, :], base_parts[:, s % 2, q * 512:(q + 1) * 512],
                                       start=True, stop=False, skip_group_check=True)
                        if q == 3:
                            mm.then_inc(parts_used, 1)
                        for u in range(2):
                            mm = pe.matmul(bank[q][u * M:(u + 1) * M, 0, :], g_blocks[:, :, :].rearrange("p b r -> p (b r)"),
                                           units[:, s, u, q * 512:(q + 1) * 512], start=False, stop=True, skip_group_check=True)
                        mm.then_inc(mix_done, 1)

                for s in range(RING):
                    pair(0, s)
                    if s == 0:
                        biases()
                with pe.Fori(1, PAIRS // RING) as it:
                    for s in range(RING):
                        pair(it, s)

            @block.scalar
            def _(act):
                act.sem_inc(act_done, 2)
                act.wait_ge(g_psum, 1)
                act.activation(g_rows[:, :], bank[0][:, 0, 0:BATCH], ACT.Identity, bias=bias_rows[:, :], scale=1.0 / SEQ)\
                   .then_inc(g_rows_done, 1)
                act.activation(g[:, :], bank[0][0:EX, 1, 0:BATCH], ACT.Identity, bias=bias[:, :], scale=1.0 / SEQ)\
                   .then_inc(g_done, 1)
                act.wait_ge(g_done, 1)
                for b in range(BATCH):
                    act.activation(g_wide[:, b, :], g[:, b:b + 1].to_broadcast([EX, P]), ACT.Copy).then_inc(g_wide_done, 1)

                def split(it, s):
                    slot = s % RING
                    act.wait_ge(unit_loaded[slot], 48 * (it + s // RING + 1))
                    act.wait_ge(parts_used, RING * it + s + 1)
                    act.activation(base_parts[0:2 * R, s % 2, :], base_rows[:, slot, :], ACT.Copy).then_inc(base_hi_done, 1)

                def pair(it, s, more=True):
                    i = RING * it + s
                    if more:
                        split(it, s + 1)
                    for q in range(2):
                        if q == 0:
                            act.wait_ge(stored[s % 2], 128 * (2 * it + s // 2 + 1))
                        act.wait_ge(mix_done, 4 * i + q + 1)
                        act.activation(mixed[:, s % 2, q * 512:(q + 1) * 512], bank[q][:, 0, :], ACT.Copy).then_inc(act_done, 1)

                split(0, 0)
                with act.Fori(0, PAIRS // RING - 1) as it:
                    for s in range(RING):
                        pair(it, s)
                for s in range(RING):
                    pair(PAIRS // RING - 1, s, more=s < RING - 1)

            @block.vector
            def _(dve):
                dve.sem_inc(dve_done, 2)
                for s in stored:
                    dve.sem_inc(s, 16 * 2 * BATCH)
                dve.wait_ge(small_loaded, 16 * 9)
                dve.tensor_copy(pick[:, :], pick_in[:, :])
                dve.tensor_copy(w2_wide[:, :, :, :], w2[:, :, :].unsqueeze(3).to_broadcast([P, KD, EX, R])).then_inc(wide_done, 1)
                dve.tensor_reduce(b_sum[:, :, :], gate_sum[:, :, :].rearrange("p k (b c) -> p k b c", b=BATCH),
                                  AX_X, ALU.add).then_inc(sum_done, 1)
                dve.wait_ge(g_rows_done, 1)
                for b in range(BATCH):
                    last = dve.tensor_scalar(g_blocks[:, b, :], mask[:, :], g_rows[:, b:b + 1], None, ALU.mult)
                last.then_inc(g_blocks_done, 1)

                def biases():
                    dve.wait_ge(bias_psum, 1)
                    for b in range(BATCH):
                        last = dve.tensor_tensor(mb1[:, b, :],
                                                 bank[0][:, 1, 0:BATCH * FF // P].rearrange("p (j b) -> p b j", b=BATCH)[:, b, :],
                                                 b1_sb[:, :], ALU.add)
                    last.then_inc(bias_done, 1)
                    for b in range(BATCH):
                        dve.wait_ge(bias_psum, b + 2)
                        dve.tensor_tensor(mb2[:, b, :], bank[(b + 1) % 4][:, 1, :], b2_sb[:, :], ALU.add)

                def split(it, s):
                    dve.wait_ge(base_hi_done, RING * it + s + 1)
                    dve.tensor_tensor(base_parts[2 * R:4 * R, s % 2, :], base_rows[:, s % RING, :],
                                      base_parts[0:2 * R, s % 2, :], ALU.subtract).then_inc(base_lo_done, 1)

                def pair(it, s, more=True):
                    i = RING * it + s
                    if more:
                        split(it, s + 1)
                    for q in range(2, 4):
                        if q == 2:
                            dve.wait_ge(stored[s % 2], 128 * (2 * it + s // 2 + 1))
                        dve.wait_ge(mix_done, 4 * i + q + 1)
                        dve.tensor_copy(mixed[:, s % 2, q * 512:(q + 1) * 512], bank[q][:, 0, :]).then_inc(dve_done, 1)

                split(0, 0)
                for s in range(RING):
                    pair(0, s)
                    if s == 0:
                        biases()
                with dve.Fori(1, PAIRS // RING - 1) as it:
                    for s in range(RING):
                        pair(it, s)
                for s in range(RING):
                    pair(PAIRS // RING - 1, s, more=s < RING - 1)


def phase_ffn(nc, mix_dram, yt_dram, x1_dram, mb1, mb2, out):
    KD = D // P
    BLOCKS = FF // P
    PER = SEQ // CH
    with ExitStack() as ctx:
        def sb(name, shape, dt):
            return ctx.enter_context(nc.sbuf_tensor("e_" + name, shape, dt))

        def sem(name):
            return nc.alloc_semaphore("e_" + name)

        w1_hi = sb("w1_hi", [P, BLOCKS, KD, P], F32R)
        w1_lo = sb("w1_lo", [P, BLOCKS, KD, P], F32R)
        w2_hi = sb("w2_hi", [P, BLOCKS, D], F32R)
        w2_lo = sb("w2_lo", [P, BLOCKS, D], F32R)
        part = sb("part", [P, 2, 2, D], F32)
        yt = sb("yt", [P, KD, CH], F32)
        y_hi = sb("y_hi", [P, KD, CH], F32R)
        y_lo = sb("y_lo", [P, KD, CH], F32R)
        u = sb("u", [P, 2, CH], F32)
        u_hi = sb("u_hi", [P, 2, CH], F32R)
        u_lo = sb("u_lo", [P, 2, CH], F32R)
        eps = sb("eps", [P, 1], F32)
        rows = sb("rows", [P, TILES, D], F32)
        x1 = sb("x1", [P, TILES, D], F32)
        stats = sb("stats", [P, TILES, 6], F32)
        moments = sb("moments", [P, TILES, 2], F32)
        std = sb("std", [P, TILES], F32)
        rstd = sb("rstd", [P, TILES], F32)
        hid = [ctx.enter_context(nc.psum_tensor(f"e_hid{i}", [P, CH], F32)) for i in range(4)]
        acc = [ctx.enter_context(nc.psum_tensor(f"e_acc{i}", [P, D], F32)) for i in range(TILES)]

        const_done = sem("const_done")
        y_loaded = sem("y_loaded")
        y_hi_done = sem("y_hi_done")
        y_lo_done = sem("y_lo_done")
        w_loaded = [sem(f"w_loaded{i}") for i in range(2)]
        w_hi_done = sem("w_hi_done")
        w_lo_done = sem("w_lo_done")
        hid_done = sem("hid_done")
        hid_seen = sem("hid_seen")
        gelu_done = sem("gelu_done")
        u_hi_done = sem("u_hi_done")
        u_lo_done = sem("u_lo_done")
        used = sem("used")
        rows_done = sem("rows_done")
        stats_chain = sem("stats_chain")
        stats_seen = sem("stats_seen")
        stats_done = sem("stats_done")
        std_done = sem("std_done")
        rstd_done = sem("rstd_done")
        norm_done = sem("norm_done")
        x1_loaded = sem("x1_loaded")
        added = sem("added")
        added_seen = sem("added_seen")
        out_stored = sem("out_stored")
        rows_free = sem("rows_free")

        def chunks(eng, chunk):
            chunk(0, 0, 0)
            with eng.Fori(0, BATCH - 1) as b:
                for q in range(1, PER + 1):
                    chunk(PER * b + q, b + q // PER, q % PER)
            for q in range(1, PER):
                chunk(PER * (BATCH - 1) + q, BATCH - 1, q)

        def final(c):
            return isinstance(c, int) and c == BATCH * PER - 1

        def turning(b, q):
            return q == PER - 1 and not (isinstance(b, int) and b == BATCH - 1)

        def first(c):
            return isinstance(c, int) and c == 0

        with nc.Block() as block:
            @block.sync
            def _(sp):
                def load_y(c):
                    cols = slice(0, CH) if isinstance(c, int) and c == 0 else bass.ds(c * CH, CH)
                    sp.dma_start(yt[:, :, :], yt_dram[:, cols].rearrange("(k p) t -> p k t", p=P)).then_inc(y_loaded, 16)

                def load_weights(b, j):
                    if not first(b) or j >= 2:
                        sp.wait_ge(w_lo_done, 2 * (BLOCKS * b + j - 1))
                    sp.dma_start(part[:, j % 2], block_of(b, j)).then_inc(w_loaded[j % 2], 16)

                def block_of(b, j):
                    n = 2 * P * D // FF
                    batch = mix_dram[0:1] if first(b) else mix_dram[bass.ds(b, 1)]
                    return batch[:, j * n:(j + 1) * n, :].rearrange("b (w r) (s h) -> (b r s) w h", w=2, h=D)

                def chunk(c, b, q):
                    if not final(c):
                        sp.wait_ge(y_lo_done, KD * (c + 1))
                        load_y(c + 1)
                    if turning(b, q):
                        for j in range(BLOCKS):
                            load_weights(b + 1, j)

                load_y(0)
                for j in range(BLOCKS):
                    load_weights(0, j)
                chunks(sp, chunk)

            @block.gpsimd
            def _(pool):
                pool.memset(eps[:, :], EPS).then_inc(const_done, 1)

                def chunk(c, b, q):
                    tokens = bass.ds(c * CH, CH)
                    pool.wait_ge(added, TILES * (c + 1))
                    pool.dma_start(x1[:, :, :], x1_dram[tokens, :].rearrange("(t p) d -> p t d", p=P)).then_inc(x1_loaded, 16)
                    pool.wait_ge(x1_loaded, 16 * (c + 1))
                    for t in range(TILES):
                        pool.wait_ge(norm_done, TILES * c + t + 1)
                        pool.tensor_tensor(rows[:, t, :], rows[:, t, :], x1[:, t, :], ALU.add).then_inc(added, 1)
                    pool.wait_ge(added, TILES * (c + 2))
                    pool.sem_inc(added_seen, 1)
                    pool.dma_start(out[tokens, :].rearrange("(t p) d -> p t d", p=P), rows[:, :, :]).then_inc(out_stored, 16)
                    pool.wait_ge(out_stored, 16 * (c + 1))
                    pool.sem_inc(rows_free, 1)

                pool.sem_inc(added, TILES)
                chunks(pool, chunk)
                pool.wait_ge(out_stored, 16 * BATCH * PER)

            @block.tensor
            def _(pe):
                pe.sem_inc(used, 2)

                def hidden(c, b, q, j):
                    n = BLOCKS * c + j
                    if q == 0:
                        pe.wait_ge(w_lo_done, 2 * BLOCKS * b + 2 * j + 1)
                    pe.wait_ge(gelu_done, n + 1)
                    for k in range(KD):
                        if j == 0:
                            pe.wait_ge(y_lo_done, KD * c + k + 1)
                        pe.matmul(hid[j % 4][:, :], w1_hi[:, j, k, :], y_hi[:, k, :], start=(k == 0), stop=False)
                        pe.matmul(hid[j % 4][:, :], w1_hi[:, j, k, :], y_lo[:, k, :], start=False, stop=False)
                        mm = pe.matmul(hid[j % 4][:, :], w1_lo[:, j, k, :], y_hi[:, k, :], start=False, stop=(k == KD - 1))
                    mm.then_inc(hid_done, 1)

                def project(c, b, q, j):
                    n = BLOCKS * c + j
                    if q == 0:
                        pe.wait_ge(w_lo_done, 2 * BLOCKS * b + 2 * j + 2)
                    pe.wait_ge(u_lo_done, n + 3)
                    for t in range(TILES):
                        cols = slice(t * P, (t + 1) * P)
                        if j == 0:
                            pe.wait_ge(rows_done, TILES * c + t + 1)
                        pe.matmul(acc[t][:, :], u_hi[:, j % 2, cols], w2_hi[:, j, :], start=(j == 0), stop=False)
                        pe.matmul(acc[t][:, :], u_hi[:, j % 2, cols], w2_lo[:, j, :], start=False, stop=False)
                        mm = pe.matmul(acc[t][:, :], u_lo[:, j % 2, cols], w2_hi[:, j, :], start=False, stop=(j == BLOCKS - 1))
                    mm.then_inc(used, 1)

                def chunk(c, b, q):
                    hidden(c, b, q, 0)
                    for j in range(1, BLOCKS):
                        hidden(c, b, q, j)
                        project(c, b, q, j - 1)
                    project(c, b, q, BLOCKS - 1)

                chunks(pe, chunk)

            def order(hidden_block, split_y, new_weights, rows_out, rows_stats, rows_norm):
                def chunk(c, b, q):
                    for j in range(0 if first(c) else 3, BLOCKS):
                        if first(c) and j + 2 < BLOCKS:
                            new_weights(0, j + 2)
                        hidden_block(c, b, j)
                        if turning(b, q):
                            if j == 3:
                                new_weights(b + 1, 0)
                            new_weights(b + 1, j - 2)
                    more = not final(c)
                    after = b + 1 if q == PER - 1 else b
                    if more:
                        split_y(c + 1)
                    rows_out(c, b)
                    if more:
                        hidden_block(c + 1, after, 0)
                    if turning(b, q):
                        new_weights(b + 1, BLOCKS - 2)
                        new_weights(b + 1, BLOCKS - 1)
                    if more:
                        hidden_block(c + 1, after, 1)
                    rows_stats(c)
                    if more:
                        hidden_block(c + 1, after, 2)
                    rows_norm(c)
                return chunk

            @block.scalar
            def _(act):
                act.sem_inc(gelu_done, 4)
                act.wait_ge(const_done, 1)

                def split_y(c):
                    act.wait_ge(y_loaded, 16 * (c + 1))
                    if not first(c):
                        act.wait_ge(hid_done, BLOCKS * c)
                    for k in range(KD):
                        act.activation(y_hi[:, k, :], yt[:, k, :], ACT.Copy).then_inc(y_hi_done, 1)

                def hidden_block(c, b, j):
                    n = BLOCKS * c + j
                    act.wait_ge(hid_done, n + 1)
                    act.wait_ge(u_lo_done, n + 1)
                    act.sem_inc(hid_seen, 1)
                    if isinstance(b, int):
                        bias = mb1[:, b, j:j + 1]
                    else:
                        bias = mb1[:, :, :].rearrange("p b j -> p (b j)")[:, bass.ds(b * BLOCKS + j, 1)]
                    act.activation(u[:, j % 2, :], hid[j % 4][:, :], ACT.Gelu_apprx_tanh, bias=bias).then_inc(gelu_done, 1)
                    act.wait_ge(gelu_done, n + 5)
                    act.wait_ge(used, n + 1)
                    act.activation(u_hi[:, j % 2, :], u[:, j % 2, :], ACT.Copy).then_inc(u_hi_done, 1)

                def new_weights(b, j):
                    act.wait_ge(w_loaded[j % 2], 16 * (BLOCKS // 2 * b + j // 2 + 1))
                    if not first(b):
                        act.wait_ge(hid_done, BLOCKS * (PER * b - 1) + j + 1)
                    act.activation(w1_hi[:, j].rearrange("p k f -> p (k f)"), part[:, j % 2, 0, :],
                                   ACT.Copy).then_inc(w_hi_done, 1)
                    if not first(b):
                        act.wait_ge(used, 2 + BLOCKS * (PER * b - 1) + j + 1)
                    act.activation(w2_hi[:, j], part[:, j % 2, 1, :], ACT.Copy).then_inc(w_hi_done, 1)

                def rows_out(c, b):
                    pass

                def rows_stats(c):
                    act.wait_ge(stats_done, c + 1)
                    act.activation(std[:, :], moments[:, :, 1], ACT.Sqrt, bias=eps[:, :]).then_inc(std_done, 1)

                def rows_norm(c):
                    pass

                split_y(0)
                new_weights(0, 0)
                new_weights(0, 1)
                chunks(act, order(hidden_block, split_y, new_weights, rows_out, rows_stats, rows_norm))

            @block.vector
            def _(dve):
                dve.sem_inc(u_lo_done, 2)
                dve.sem_inc(rows_done, TILES)
                dve.sem_inc(rows_free, 1)

                def split_y(c):
                    for k in range(KD):
                        dve.wait_ge(y_hi_done, KD * c + k + 1)
                        dve.tensor_tensor(y_lo[:, k, :], yt[:, k, :], y_hi[:, k, :], ALU.subtract).then_inc(y_lo_done, 1)

                def hidden_block(c, b, j):
                    n = BLOCKS * c + j
                    dve.wait_ge(u_hi_done, n + 1)
                    dve.tensor_tensor(u_lo[:, j % 2, :], u[:, j % 2, :], u_hi[:, j % 2, :], ALU.subtract).then_inc(u_lo_done, 1)

                def new_weights(b, j):
                    for which, (hi, lo) in enumerate(((w1_hi, w1_lo), (w2_hi, w2_lo))):
                        dve.wait_ge(w_hi_done, 2 * (BLOCKS * b + j) + which + 1)
                        dst, high = (m[:, j].rearrange("p k f -> p (k f)") if which == 0 else m[:, j] for m in (lo, hi))
                        dve.tensor_tensor(dst, part[:, j % 2, which, :], high, ALU.subtract).then_inc(w_lo_done, 1)

                def rows_out(c, b):
                    dve.wait_ge(rows_free, c + 1)
                    dve.wait_ge(used, 2 + BLOCKS * (c + 1))
                    for t in range(TILES):
                        bias = mb2[:, b, :] if isinstance(b, int) else \
                            mb2[:, :, :].rearrange("p b d -> p (b d)")[:, bass.ds(b * D, D)]
                        dve.tensor_tensor(rows[:, t, :], acc[t][:, :], bias, ALU.add).then_inc(rows_done, 1)

                def rows_stats(c):
                    dve.wait_ge(rows_done, TILES * (c + 2))
                    for t in range(TILES):
                        dve.bn_stats(stats[:, t, :], rows[:, t, :]).then_inc(stats_chain, 1)
                    dve.wait_ge(stats_chain, TILES * (c + 1))
                    dve.sem_inc(stats_seen, 1)
                    for t in range(TILES):
                        last = dve.bn_aggr(moments[:, t, :], stats[:, t, :])
                    last.then_inc(stats_done, 1)

                def rows_norm(c):
                    dve.wait_ge(std_done, c + 1)
                    dve.reciprocal(rstd[:, :], std[:, :]).then_inc(rstd_done, 1)
                    dve.wait_ge(rstd_done, c + 1)
                    for t in range(TILES):
                        dve.tensor_scalar(rows[:, t, :], rows[:, t, :], moments[:, t, 0:1], rstd[:, t:t + 1],
                                          ALU.subtract, ALU.mult).then_inc(norm_done, 1)

                split_y(0)
                new_weights(0, 0)
                new_weights(0, 1)
                chunks(dve, order(hidden_block, split_y, new_weights, rows_out, rows_stats, rows_norm))


def attention_and_mixed_ffn(nc, x, w_qkv, gate_w1, gate_b1, gate_w2, gate_b2_rows, gate_b2, b1, b2, tb1, tb2, mask_rows, pick_rows,
                            base, experts, out):
    def scratch(name, shape):
        return nc.dram_tensor(name, shape, F32, kind="Internal").ap()

    qk_dram = scratch("qk_scratch", [2, 2, P, QUADS, TOKENS])
    v_dram = scratch("v_scratch", [QUADS, TOKENS, QH * E])
    o_dram = scratch("o_scratch", [QUADS, TOKENS, QH * E])
    x1_dram = scratch("x1_scratch", [TOKENS, D])
    yt_dram = scratch("yt_scratch", [D, TOKENS])
    mix_dram = scratch("mix_scratch", [BATCH, 2 * D, FF])
    with ExitStack() as ctx:
        gate_sum = ctx.enter_context(nc.sbuf_tensor("gate_sum", [P, D // P, CHUNKS], F32))
        mb1 = ctx.enter_context(nc.sbuf_tensor("mb1", [P, BATCH, FF // P], F32))
        mb2 = ctx.enter_context(nc.sbuf_tensor("mb2", [P, BATCH, D], F32))
        phase_qkv(nc, x, w_qkv, qk_dram, v_dram)
        with ExitStack() as middle:
            units = middle.enter_context(nc.sbuf_tensor("units", [P, SLOTS, 2, FF], F32))
            unit_loaded = [nc.alloc_semaphore(f"unit_loaded{i}") for i in range(SLOTS)]
            phase_attention(nc, qk_dram, v_dram, o_dram, unit_loader(experts, units, unit_loaded))
            phase_gate(nc, x, gate_w1, gate_b1, o_dram, x1_dram, yt_dram, gate_sum)
            phase_mix(nc, mask_rows, pick_rows, base, experts, gate_w2, gate_b2_rows, gate_b2, b1, b2, tb1, tb2, gate_sum,
                      units, unit_loaded, mix_dram, mb1, mb2)
        phase_ffn(nc, mix_dram, yt_dram, x1_dram, mb1, mb2, out)


def kernel(**inputs):
    import numpy as np
    import concourse.bacc as bacc
    from concourse.bass_utils import run_bass_kernel_spmd

    a = {name.replace("L0_attn_", "").replace("L0_ffn_", ""): np.asarray(value) for name, value in inputs.items()}
    rows = P // EXPERTS

    def blocks(w1, w2):
        lead, n = w1.shape[:-2], FF // P
        w1 = np.moveaxis(w1.reshape(*lead, n, P, D // P, P), (-1, -2, -3), (-3, -2, -1))
        w2 = np.swapaxes(w2, -1, -2)
        both = [w.reshape(*lead, n, P * D // FF, FF) for w in (w1, w2)]
        return np.concatenate(both, -2).reshape(*lead, 2 * D, FF)

    experts = blocks(a["TW1"], a["TW2"]).reshape(EXPERTS, 2 * D // rows, rows, FF).transpose(1, 0, 2, 3)
    laid_out = {
        "x": a["x"].reshape(TOKENS, D),
        "w_qkv": a["w_qkv"],
        "gate_w1": a["gate_w1"].T,
        "gate_b1": a["gate_b1"].reshape(D // P, P).T,
        "gate_w2": a["gate_w2"].T,
        "gate_b2_rows": np.repeat(a["gate_b2"], rows)[:, None],
        "gate_b2": a["gate_b2"][:, None],
        "b1": a["b1"].reshape(FF // P, P).T,
        "b2": np.tile(a["b2"][None, :], (P, 1)),
        "tb1": a["Tb1"],
        "tb2": a["Tb2"],
        "mask_rows": np.tile(np.eye(rows, dtype=np.float32), (EXPERTS, 1)),
        "pick_rows": np.tile(np.kron(np.eye(2, dtype=np.float32), np.tile(np.eye(rows, dtype=np.float32), (1, BATCH))), (2, 1)),
        "base": blocks(a["W1"], a["W2"]),
        "experts": experts.reshape(2 * D // rows, P, FF),
    }
    nc = bacc.Bacc("TRN2", target_bir_lowering=False, num_devices=1)
    arrays, args = {}, []
    for name, value in laid_out.items():
        arrays[name] = np.ascontiguousarray(value)
        args.append(nc.dram_tensor(name, arrays[name].shape, mybir.dt.from_np(arrays[name].dtype), kind="ExternalInput").ap())
    args.append(nc.dram_tensor("out", (TOKENS, D), F32, kind="ExternalOutput").ap())
    attention_and_mixed_ffn(nc, *args)
    result = run_bass_kernel_spmd(nc, [arrays], core_ids=[0])
    return result.results[0]["out"].reshape(BATCH, SEQ, D)
```
